# Optimizing a Trainium2 kernel written in Bass

```python
import numpy as np
import jax
import jax.numpy as jnp

def _softmax(x, axis=-1):
    return jax.nn.softmax(x, axis=axis)

def _gelu(x):
    return jax.nn.gelu(x, approximate=True)

def _silu(x):
    return jax.nn.silu(x)

def _sigmoid(x):
    return jax.nn.sigmoid(x)

def _layernorm(x, axis=-1, eps=1e-05):
    m = jnp.mean(x, axis=axis, keepdims=True)
    v = jnp.var(x, axis=axis, keepdims=True)
    return (x - m) / jnp.sqrt(v + eps)

def _scatter_add(tgt, idx, src, axis=0):
    return tgt.at[idx].add(src)

def _segment_sum(src, seg, n):
    return jax.ops.segment_sum(src, seg, n)
kernel_name = 'mk_rec_standalone_d1_rec_r8_6da5a6'

def setup_inputs(seed: int=0):
    np.random.seed(seed)
    _w = jnp.asarray

    def _rec_inputs():
        import jax
        import jax.numpy as jnp
        _rk = jax.random.key(seed)
        r_x = -0.000125008 + 0.999885 * jax.random.normal(jax.random.fold_in(_rk, 1), (512, 64, 128), jnp.float32)
        return r_x
    r_x = _rec_inputs()

    def _L0_rec_setup():
        import jax, jax.numpy as jnp
        import numpy as np
        B, N, D = (512, 64, 128)
        H, ATT = (8, 32)
        SCALE = ATT ** (-0.5)
        key = jax.random.key(seed)
        k1, k2, k3, k4, k5 = jax.random.split(key, 5)
        x = jax.random.normal(k1, (B, N, D), dtype=jnp.float32)
        W_Q = jax.random.normal(k2, (H, D, ATT), dtype=jnp.float32) * (2.0 / (D + ATT)) ** 0.5
        W_K = jax.random.normal(k3, (H, D, ATT), dtype=jnp.float32) * (2.0 / (D + ATT)) ** 0.5
        W_V = jax.random.normal(k4, (H, D, ATT), dtype=jnp.float32) * (2.0 / (D + ATT)) ** 0.5
        W_res = jax.random.normal(k5, (D, H * ATT), dtype=jnp.float32) * (2.0 / (D + H * ATT)) ** 0.5
        return {'x': x, 'W_Q': W_Q, 'W_K': W_K, 'W_V': W_V, 'W_res': W_res}
    _L0_rec_all = _L0_rec_setup()
    _L0_rec_in = {k: v for k, v in _L0_rec_all.items() if k in ('W_Q', 'W_K', 'W_V', 'W_res')}
    del _L0_rec_all
    return {'r_x': r_x, 'L0_rec_W_Q': _L0_rec_in['W_Q'], 'L0_rec_W_K': _L0_rec_in['W_K'], 'L0_rec_W_V': _L0_rec_in['W_V'], 'L0_rec_W_res': _L0_rec_in['W_res']}

def reference(r_x, L0_rec_W_Q, L0_rec_W_K, L0_rec_W_V, L0_rec_W_res):
    import jax
    import jax.numpy as jnp

    def _L0_rec_ref(x, W_Q, W_K, W_V, W_res):
        import jax, jax.numpy as jnp
        import numpy as np
        B, N, D = (512, 64, 128)
        H, ATT = (8, 32)
        SCALE = ATT ** (-0.5)
        Q = jnp.einsum('bnd,hdk->bhnk', x, W_Q)
        K = jnp.einsum('bnd,hdk->bhnk', x, W_K)
        V = jnp.einsum('bnd,hdk->bhnk', x, W_V)
        scores = jnp.einsum('bhnk,bhmk->bhnm', Q, K) * SCALE
        attn = jax.nn.softmax(scores, axis=-1)
        ctx = jnp.einsum('bhnm,bhmk->bhnk', attn, V)
        ctx = ctx.transpose(0, 2, 1, 3).reshape(x.shape[0], x.shape[1], H * ATT)
        res = x @ W_res
        return jax.nn.relu(ctx + res)
    y = _L0_rec_ref(r_x, L0_rec_W_Q, L0_rec_W_K, L0_rec_W_V, L0_rec_W_res)
    return y

_drawn_inputs = setup_inputs


def setup_inputs(seed=0):
    import zlib

    import numpy as np

    out = dict(_drawn_inputs(seed))
    spreads = {}
    factors = {}
    for name, (base, spread) in spreads.items():
        noise = np.random.default_rng([zlib.crc32(name.encode()), seed]).standard_normal(out[name].shape)
        drawn = base * np.exp(spread * noise) if base else spread * noise
        out[name] = jnp.asarray(drawn.astype(out[name].dtype))
    for name, factor in factors.items():
        out[name] = (out[name] * factor).astype(out[name].dtype)
    return out
```

```python
import concourse.bass as bass
from concourse import mybir
from contextlib import ExitStack


def build_attention_program(nc: bass.Bass, x_t: bass.AP, w_t: bass.AP, out: bass.AP):
    fp32 = mybir.dt.float32
    fp32r = mybir.dt.float32r
    ALU = mybir.AluOpType
    ACT = mybir.ActivationFunctionType
    AX = mybir.AxisListType

    D, TOKENS = x_t.shape
    F = out.shape[1]
    N, ATT = 64, 32
    H = F // ATT
    HP = H // 2
    SCALE = float(ATT) ** -0.5
    TILE = 128
    TB = TILE // N
    GT = 4
    GROUP = GT * TILE
    GROUPS = TOKENS // GROUP
    TILES = TOKENS // TILE
    CHUNKS = F // 128
    QK = 2 * CHUNKS
    PLAN = [[], [(1, 0)], [(1, 1), (0, 0)], [(0, 1)]]
    QK_BEFORE = [0, 0, 1, 3]
    IN_ORDER = [one for plan in PLAN for one in plan]
    BODY = 2 * GT
    FIRST = GT + 2
    TURNS = (TILES - GT - FIRST) // BODY

    ctx = ExitStack()
    with ctx:
        def sb(name, shape, dt=fp32):
            return ctx.enter_context(nc.sbuf_tensor(name, shape, dt))

        def bank(name):
            return ctx.enter_context(nc.psum_tensor(name, [128, 512], fp32))

        def sem(name):
            return ctx.enter_context(nc.semaphore(name))

        w_in = sb("w_in", [128, 4 * F])
        w_hi = sb("w_hi", [128, 4 * F], fp32r)
        w_lo = sb("w_lo", [128, 4 * F], fp32r)
        x_in = [sb(f"x_in{p}", [128, GROUP]) for p in range(2)]
        x_hi = [sb(f"x_hi{p}", [128, GROUP], fp32r) for p in range(2)]
        x_lo = [sb(f"x_lo{p}", [128, GROUP], fp32r) for p in range(2)]
        qT = [sb(f"qT{p}", [128, CHUNKS, GROUP]) for p in range(2)]
        kT = [sb(f"kT{p}", [128, CHUNKS, 2, GROUP]) for p in range(2)]
        probs = [sb(f"probs{p}", [128, 2, H // 2, N]) for p in range(2)]
        row_max = [sb(f"row_max{p}", [128, 2, H // 2]) for p in range(2)]
        probs_t = sb("probs_t", [128, HP, TILE])
        v_blocks = [sb(f"v_blocks{p}", [128, TB, HP, 2, ATT + 1]) for p in range(2)]
        inv_sum = sb("inv_sum", [128, H])
        head_out = sb("head_out", [128, H, ATT])
        out_sb = [sb(f"out_sb{p}", [128, GT, F]) for p in range(2)]
        identity = sb("identity", [128, 128])
        parity = sb("parity", [128, 2])

        qk_bank = [bank(f"qk_bank{i}") for i in range(2)]
        score_banks = ctx.enter_context(nc.psum_tensor("score_banks", [128, 2, 512], fp32))
        score = score_banks[:, :, 0:H // 2 * N].rearrange("p r (q m) -> p r q m", m=N)
        probs_t_bank = bank("probs_t_bank")
        v_bank = bank("v_bank")
        ctx_bank = bank("ctx_bank")
        res_bank = bank("res_bank")
        ctx_psum = ctx_bank[:, 0:H * (ATT + 1)].rearrange("p (h e) -> p h e", h=H)

        w_loaded = sem("w_loaded")
        x_loaded = [sem(f"x_loaded{p}") for p in range(2)]
        stored = [sem(f"stored{p}") for p in range(2)]
        pool_steps = sem("pool_steps")
        constants = sem("constants")
        w_rounded = sem("w_rounded")
        w_split = sem("w_split")
        x_rounded = sem("x_rounded")
        x_split = sem("x_split")
        qk_projected = sem("qk_projected")
        qk_copied = sem("qk_copied")
        scores_begun = sem("scores_begun")
        scored = sem("scored")
        maxed = sem("maxed")
        scores_shifted = sem("scores_shifted")
        exped = sem("exped")
        transposed = sem("transposed")
        probs_t_copied = sem("probs_t_copied")
        v_projected = sem("v_projected")
        v_copied = sem("v_copied")
        res_projected = sem("res_projected")
        attended = sem("attended")
        inverted = sem("inverted")
        scaled = sem("scaled")
        res_added = sem("res_added")
        finished = sem("finished")

        block = ctx.enter_context(nc.Block())

        def tile(turn, s):
            return turn * BODY + s

        def group(turn, s):
            return turn * (BODY // GT) + s // GT

        LAST = ((TILES - 1) // BODY, (TILES - 1) % BODY)

        def side(s):
            return (s // GT) % 2

        def reaches(count, least):
            return not isinstance(count, int) or count >= least

        def run_tiles(eng, step):
            for t in range(FIRST):
                step(0, t)
            with eng.Fori(0, TURNS) as turn:
                for s in range(FIRST, FIRST + BODY):
                    step(turn, s)
            for t in range(FIRST + TURNS * BODY, TILES):
                step(t // BODY, t % BODY)

        @block.sync
        def _(sp):
            def load(g, p):
                sp.dma_start(x_in[p][:, :], x_t[:, bass.ds(g * GROUP, GROUP)]).then_inc(x_loaded[p], 16)

            def store(g, p):
                sp.wait_ge(finished, g * GT + GT)
                rows = out[bass.ds(g * GROUP, GROUP), :].rearrange("(t p) f -> p t f", p=TILE)
                sp.dma_start(rows, out_sb[p][:, :, :]).then_inc(stored[p], 16)

            sp.dma_start(w_in[:, :], w_t).then_inc(w_loaded, 16)
            load(0, 0)
            load(1, 1)
            with sp.Fori(0, GROUPS // 2 - 1) as turn:
                for p in range(2):
                    sp.wait_ge(x_split, turn * 2 + (p + 1))
                    load(turn * 2 + (p + 2), p)
                    store(turn * 2 + p, p)
            for p in range(2):
                store(GROUPS - 2 + p, p)
            for p in range(2):
                sp.wait_ge(stored[p], 16 * (GROUPS // 2))

        @block.gpsimd
        def _(pool):
            count = 0

            def in_turn(instruction):
                nonlocal count
                count += 1
                instruction.then_inc(pool_steps, 1)
                pool.wait_ge(pool_steps, count)

            in_turn(nc.gpsimd.memset(identity[:, :], 0.0))
            in_turn(nc.gpsimd.memset(parity[:, :], 0.0))
            for p in range(2):
                in_turn(nc.gpsimd.memset(v_blocks[p][:, :, :, :, :], 0.0))
            in_turn(nc.gpsimd.affine_select(out=identity[:, :], in_=identity[:, :], compare_op=ALU.not_equal,
                                            fill=1.0, base=0, pattern=[[-1, 128]], channel_multiplier=1))
            for q in range(4):
                in_turn(nc.gpsimd.memset(parity[32 * q:32 * q + 32, q % 2:q % 2 + 1], 1.0))
            for p in range(2):
                for j in range(2):
                    last = nc.gpsimd.memset(v_blocks[p][64 * j:64 * j + 64, :, :, j, ATT:ATT + 1], 1.0)
                    if (p, j) != (1, 1):
                        in_turn(last)
            last.then_inc(constants, 1)

        @block.tensor
        def _(pe):
            def three_products(psum, w_cols, x_cols, p, x_stationary):
                for n, (w, x) in enumerate(((w_lo, x_hi[p]), (w_hi, x_lo[p]), (w_hi, x_hi[p]))):
                    stationary, moving = w[:, w_cols], x[:, x_cols]
                    if x_stationary:
                        stationary, moving = moving, stationary
                    last = nc.tensor.matmul(psum, stationary, moving, start=(n == 0), stop=(n == 2))
                return last

            def project_qk(turn, s, done, is_k, c):
                g = group(turn, s)
                pe.wait_ge(x_split, g + 1)
                if reaches(g, 1) or done >= 2:
                    pe.wait_ge(qk_copied, g * QK + (done - 1))
                col = is_k * F + c * 128
                three_products(qk_bank[done % 2][:, :], slice(col, col + 128), slice(0, GROUP),
                               side(s), False).then_inc(qk_projected, 1)

            def scores(turn, s):
                p, u, t = side(s), s % GT, tile(turn, s)
                if u == 0:
                    pe.wait_ge(qk_copied, group(turn, s) * QK + QK)
                if reaches(t, 1):
                    pe.wait_ge(scores_shifted, t)
                pe.sem_inc(scores_begun, 1)
                for c in range(CHUNKS):
                    for b in range(TB):
                        tok = slice(u * TILE + b * N, u * TILE + b * N + N)
                        for r in range(2):
                            rows = slice(64 * r, 64 * r + 64)
                            last = nc.tensor.matmul(
                                score[64 * b:64 * b + 64, r, 2 * c:2 * c + 2, :],
                                qT[p][rows, c, tok], kT[p][rows, c, :, tok], start=True, stop=True)
                last.then_inc(scored, 1)

            def transposes(turn, s):
                pe.wait_ge(exped, tile(turn, s) + 1)
                for hp in range(HP):
                    last = nc.tensor.transpose(probs_t_bank[:, 128 * hp:128 * hp + 128],
                                               probs[s % 2][:, hp % 2, hp // 2 * 2:hp // 2 * 2 + 2, :].rearrange("p j m -> p (j m)"),
                                               identity[:, :])
                last.then_inc(transposed, 1)

            def project_v(turn, s):
                t, u = tile(turn, s), s % GT
                if reaches(t, 1):
                    pe.wait_ge(v_copied, t)
                three_products(v_bank[:, 0:F], slice(2 * F, 3 * F), slice(u * TILE, u * TILE + TILE),
                               side(s), True).then_inc(v_projected, 1)

            def project_res(turn, s):
                t, u = tile(turn, s), s % GT
                if reaches(t, 1):
                    pe.wait_ge(res_added, t)
                three_products(res_bank[:, 0:F], slice(3 * F, 4 * F), slice(u * TILE, u * TILE + TILE),
                               side(s), True).then_inc(res_projected, 1)

            def attend(turn, s):
                t = tile(turn, s)
                if reaches(t, 1):
                    pe.wait_ge(scaled, t)
                pe.wait_ge(v_copied, t + 1)
                pe.wait_ge(probs_t_copied, t + 1)
                for b in range(TB):
                    for hp in range(HP):
                        last = nc.tensor.matmul(
                            ctx_psum[64 * b:64 * b + 64, 2 * hp:2 * hp + 2, :],
                            probs_t[:, hp, 64 * b:64 * b + 64], v_blocks[s % 2][:, b, hp, :, :],
                            start=True, stop=True)
                last.then_inc(attended, 1)

            def step(turn, s):
                scores(turn, s)
                if not isinstance(turn, int) or group(turn, s) + 1 < GROUPS:
                    for n, (is_k, c) in enumerate(PLAN[s % GT]):
                        project_qk(turn, s + GT, QK_BEFORE[s % GT] + n, is_k, c)
                more = reaches(tile(turn, s), 1)
                if more:
                    transposes(turn, s - 1)
                project_v(turn, s)
                if more:
                    project_res(turn, s - 1)
                    attend(turn, s - 1)

            pe.wait_ge(constants, 1)
            pe.wait_ge(w_split, 1)
            for n, (is_k, c) in enumerate(IN_ORDER):
                project_qk(0, 0, n, is_k, c)
            run_tiles(pe, step)
            transposes(*LAST)
            project_res(*LAST)
            attend(*LAST)

        @block.scalar
        def _(act):
            def copy_qk(turn, s, done, is_k, c):
                g, p = group(turn, s), side(s)
                act.wait_ge(qk_projected, g * QK + (done + 1))
                if done == 0 and reaches(g, 2):
                    act.wait_ge(scored, g * GT - GT)
                if is_k:
                    for j in range(2):
                        last = nc.scalar.activation(kT[p][:, c, j, :], qk_bank[done % 2][:, :], ACT.Copy,
                                                    scale=parity[:, j:j + 1])
                else:
                    last = nc.scalar.activation(qT[p][:, c, :], qk_bank[done % 2][:, :], ACT.Copy)
                last.then_inc(qk_copied, 1)

            def copy_probs_t(turn, s):
                act.wait_ge(transposed, tile(turn, s) + 1)
                nc.scalar.activation(probs_t[:, :, :], probs_t_bank[:, :].rearrange("p (c n) -> p c n", c=HP),
                                     ACT.Copy).then_inc(probs_t_copied, 1)

            def copy_v(turn, s):
                t = tile(turn, s)
                act.wait_ge(v_projected, t + 1)
                if reaches(t, 2):
                    act.wait_ge(attended, t - 1)
                for b in range(TB):
                    v = v_bank[64 * b:64 * b + 64, 0:F].rearrange("p (c j k) -> p j c k", c=HP, j=2)
                    for j in range(2):
                        last = nc.scalar.activation(v_blocks[s % 2][64 * j:64 * j + 64, b, :, j, 0:ATT],
                                                    v[:, j, :, :], ACT.Copy)
                last.then_inc(v_copied, 1)

            def exp(turn, s):
                t = tile(turn, s)
                act.wait_ge(scores_shifted, t + 1)
                nc.scalar.activation(probs[s % 2][:, :, :, :], probs[s % 2][:, :, :, :], ACT.Exp,
                                     scale=SCALE).then_inc(exped, 1)

            def step(turn, s):
                todo = []
                if not isinstance(turn, int) or group(turn, s) + 1 < GROUPS:
                    todo = [(QK_BEFORE[s % GT] + n, is_k, c) for n, (is_k, c) in enumerate(PLAN[s % GT])]
                for what in todo:
                    if what[0] == QK - 1:
                        copy_qk(turn, s + GT, *what)
                if reaches(tile(turn, s), 1):
                    copy_probs_t(turn, s - 1)
                copy_v(turn, s)
                exp(turn, s)
                for what in todo:
                    if what[0] != QK - 1:
                        copy_qk(turn, s + GT, *what)

            act.wait_ge(constants, 1)
            for n, (is_k, c) in enumerate(IN_ORDER):
                copy_qk(0, 0, n, is_k, c)
            run_tiles(act, step)
            copy_probs_t(*LAST)

        @block.vector
        def _(dve):
            def split_x(turn, s):
                g, p = group(turn, s), side(s)
                dve.wait_ge(x_loaded[p], turn * 16 + (s // BODY) * 16 + 16)
                if reaches(g, 2):
                    dve.wait_ge(res_projected, g * GT - GT)
                nc.vector.tensor_copy(x_hi[p][:, :], x_in[p][:, :]).then_inc(x_rounded, 1)
                dve.wait_ge(x_rounded, g + 1)
                nc.vector.tensor_tensor(x_lo[p][:, :], x_in[p][:, :], x_hi[p][:, :].bitcast(fp32),
                                        ALU.subtract).then_inc(x_split, 1)

            def shift(turn, s):
                t = tile(turn, s)
                dve.wait_ge(scored, t + 1)
                most = row_max[s % 2][:, :, :]
                nc.vector.tensor_reduce(out=most, in_=score, axis=AX.X, op=ALU.max).then_inc(maxed, 1)
                dve.wait_ge(maxed, t + 1)
                if reaches(t, 2):
                    dve.wait_ge(transposed, t - 1)
                nc.vector.tensor_tensor(probs[s % 2][:, :, :, :], score,
                                        most.unsqueeze(3).to_broadcast([128, 2, H // 2, N]),
                                        ALU.subtract).then_inc(scores_shifted, 1)

            def finish(turn, s):
                t, p, u = tile(turn, s), side(s), s % GT
                dve.wait_ge(attended, t + 1)
                nc.vector.reciprocal(inv_sum[:, :], ctx_psum[:, :, ATT]).then_inc(inverted, 1)
                dve.wait_ge(inverted, t + 1)
                nc.vector.tensor_tensor(head_out[:, :, :], ctx_psum[:, :, 0:ATT],
                                        inv_sum[:, :].unsqueeze(2).to_broadcast([128, H, ATT]),
                                        ALU.mult).then_inc(scaled, 1)
                if u == 0 and reaches(t, 2 * GT):
                    dve.wait_ge(stored[p], turn * 16 + (s // BODY) * 16)
                dve.wait_ge(scaled, t + 1)
                dve.wait_ge(res_projected, t + 1)
                o = out_sb[p][:, u, :]
                nc.vector.tensor_tensor(o, res_bank[:, 0:F], head_out[:, :, :].rearrange("p h k -> p (h k)"),
                                        ALU.add).then_inc(res_added, 1)
                dve.wait_ge(res_added, t + 1)
                nc.vector.tensor_scalar(o, o, 0.0, None, ALU.max).then_inc(finished, 1)

            def step(turn, s):
                shift(turn, s)
                if s % GT == 0 and (not isinstance(turn, int) or group(turn, s) + 1 < GROUPS):
                    split_x(turn, s + GT)
                if reaches(tile(turn, s), 1):
                    finish(turn, s - 1)

            dve.wait_ge(w_loaded, 16)
            nc.vector.tensor_copy(w_hi[:, :], w_in[:, :]).then_inc(w_rounded, 1)
            dve.wait_ge(w_rounded, 1)
            nc.vector.tensor_tensor(w_lo[:, :], w_in[:, :], w_hi[:, :].bitcast(fp32),
                                    ALU.subtract).then_inc(w_split, 1)
            split_x(0, 0)
            run_tiles(dve, step)
            finish(*LAST)


def kernel(r_x, L0_rec_W_Q, L0_rec_W_K, L0_rec_W_V, L0_rec_W_res):
    import numpy as np
    import concourse.bacc as bacc
    from concourse.bass_utils import run_bass_kernel_spmd

    B, N, D = r_x.shape
    H, _, ATT = L0_rec_W_Q.shape
    F = H * ATT
    x_t = np.ascontiguousarray(np.asarray(r_x).reshape(B * N, D).transpose(1, 0))
    per_head = [np.asarray(w).transpose(1, 0, 2).reshape(D, F) for w in (L0_rec_W_Q, L0_rec_W_K, L0_rec_W_V)]
    w_t = np.ascontiguousarray(np.concatenate(per_head + [np.asarray(L0_rec_W_res)], axis=1))

    nc = bacc.Bacc("TRN2", target_bir_lowering=False, num_devices=1)
    x_dram = nc.dram_tensor("x_t", x_t.shape, mybir.dt.float32, kind="ExternalInput").ap()
    w_dram = nc.dram_tensor("w_t", w_t.shape, mybir.dt.float32, kind="ExternalInput").ap()
    out_dram = nc.dram_tensor("out", (B * N, F), mybir.dt.float32, kind="ExternalOutput").ap()
    build_attention_program(nc, x_dram, w_dram, out_dram)
    r = run_bass_kernel_spmd(nc, [{"x_t": x_t, "w_t": w_t}], core_ids=[0])
    return r.results[0]["out"].reshape(B, N, F)
```

```python
import concourse.bass as bass
from concourse import mybir
from contextlib import ExitStack


def build_attention_program(nc: bass.Bass, x_t: bass.AP, w_t: bass.AP, out: bass.AP):
    fp32 = mybir.dt.float32
    fp32r = mybir.dt.float32r
    ALU = mybir.AluOpType
    ACT = mybir.ActivationFunctionType
    AX = mybir.AxisListType

    D, TOKENS = x_t.shape
    F = out.shape[1]
    N, ATT = 64, 32
    H = F // ATT
    HP = H // 2
    SCALE = float(ATT) ** -0.5
    TILE = 128
    TB = TILE // N
    PAIR = 2 * TILE
    GT = 4
    GROUP = GT * TILE
    GROUPS = TOKENS // GROUP
    TILES = TOKENS // TILE
    CHUNKS = F // 128
    BODY = 2 * GT
    TURNS = TILES // BODY - 2
    LAST_STEP = TILES + 2

    ctx = ExitStack()
    with ctx:
        def sb(name, shape, dt=fp32):
            return ctx.enter_context(nc.sbuf_tensor(name, shape, dt))

        def bank(name):
            return ctx.enter_context(nc.psum_tensor(name, [128, 512], fp32))

        def sem(name):
            return ctx.enter_context(nc.semaphore(name))

        w_in = sb("w_in", [128, 4 * F])
        w_hi = sb("w_hi", [128, 4 * F], fp32r)
        w_lo = sb("w_lo", [128, 4 * F], fp32r)
        x_in = [sb(f"x_in{i}", [128, GROUP]) for i in range(2)]
        x_hi = [sb(f"x_hi{i}", [128, PAIR], fp32r) for i in range(4)]
        x_lo = [sb(f"x_lo{i}", [128, PAIR], fp32r) for i in range(4)]
        qT = [sb(f"qT{i}", [128, CHUNKS, PAIR]) for i in range(2)]
        kT = [sb(f"kT{i}", [128, CHUNKS, 2, PAIR]) for i in range(2)]
        probs = [sb(f"probs{i}", [128, 2, H // 2, N]) for i in range(2)]
        row_max = [sb(f"row_max{i}", [128, 2, H // 2]) for i in range(2)]
        probs_t = sb("probs_t", [128, HP, TILE])
        v_blocks = [sb(f"v_blocks{i}", [128, TB, HP, 2, ATT + 1]) for i in range(2)]
        inv_sum = sb("inv_sum", [128, H])
        head_out = sb("head_out", [128, H, ATT])
        out_sb = [sb(f"out_sb{i}", [128, GT, F]) for i in range(2)]
        identity = sb("identity", [128, 128])
        parity = sb("parity", [128, 2])

        key_bank = bank("key_bank")
        query_bank = bank("query_bank")
        score_banks = ctx.enter_context(nc.psum_tensor("score_banks", [128, 2, 512], fp32))
        probs_t_bank = bank("probs_t_bank")
        v_bank = bank("v_bank")
        ctx_bank = bank("ctx_bank")
        res_bank = bank("res_bank")
        key_psum = key_bank[:, :].rearrange("p (c n) -> p c n", c=CHUNKS)
        query_psum = query_bank[:, :].rearrange("p (c n) -> p c n", c=CHUNKS)
        score = score_banks[:, :, 0:H // 2 * N].rearrange("p r (q m) -> p r q m", m=N)
        ctx_psum = ctx_bank[:, 0:H * (ATT + 1)].rearrange("p (h e) -> p h e", h=H)

        w_loaded = [sem(f"w_loaded{i}") for i in range(2)]
        x_loaded = [sem(f"x_loaded{i}") for i in range(2)]
        stored = [sem(f"stored{i}") for i in range(2)]
        pool_steps = sem("pool_steps")
        constants = sem("constants")
        w_rounded = sem("w_rounded")
        w_split = sem("w_split")
        x_rounded = sem("x_rounded")
        x_split = sem("x_split")
        qk_projected = sem("qk_projected")
        qk_copied = sem("qk_copied")
        scores_begun = sem("scores_begun")
        scored = sem("scored")
        maxed = sem("maxed")
        scores_shifted = sem("scores_shifted")
        exped = sem("exped")
        transposed = sem("transposed")
        probs_t_copied = sem("probs_t_copied")
        v_projected = sem("v_projected")
        v_copied = sem("v_copied")
        res_projected = sem("res_projected")
        attended = sem("attended")
        inverted = sem("inverted")
        scaled = sem("scaled")
        res_added = sem("res_added")
        finished = sem("finished")

        block = ctx.enter_context(nc.Block())

        def tile(turn, s):
            return turn * BODY + s

        def pair(turn, s):
            return turn * (BODY // 2) + s // 2

        def real(turn, s):
            return not isinstance(turn, int) or 0 <= tile(turn, s) < TILES

        def reaches(count, least):
            return not isinstance(count, int) or count >= least

        def run_steps(eng, step):
            for t in range(BODY):
                step(0, t)
            with eng.Fori(1, TURNS + 1) as turn:
                for s in range(BODY):
                    step(turn, s)
            for t in range((TURNS + 1) * BODY, LAST_STEP + 1):
                step(TURNS + 1, t - (TURNS + 1) * BODY)

        @block.sync
        def _(sp):
            def load(g, i):
                sp.dma_start(x_in[i][:, :], x_t[:, bass.ds(g * GROUP, GROUP)]).then_inc(x_loaded[i], 16)

            def store(g, i):
                sp.wait_ge(finished, g * GT + GT)
                rows = out[bass.ds(g * GROUP, GROUP), :].rearrange("(t p) f -> p t f", p=TILE)
                sp.dma_start(rows, out_sb[i][:, :, :]).then_inc(stored[i], 16)

            sp.dma_start(w_in[:, 0:2 * F], w_t[:, 0:2 * F]).then_inc(w_loaded[0], 16)
            load(0, 0)
            sp.dma_start(w_in[:, 2 * F:], w_t[:, 2 * F:]).then_inc(w_loaded[1], 16)
            load(1, 1)
            with sp.Fori(0, GROUPS // 2 - 1) as turn:
                for i in range(2):
                    sp.wait_ge(x_split, turn * 4 + (2 * i + 2))
                    load(turn * 2 + (i + 2), i)
                    store(turn * 2 + i, i)
            for i in range(2):
                store(GROUPS - 2 + i, i)
            for i in range(2):
                sp.wait_ge(stored[i], 16 * (GROUPS // 2))

        @block.gpsimd
        def _(pool):
            count = 0

            def in_turn(instruction):
                nonlocal count
                count += 1
                instruction.then_inc(pool_steps, 1)
                pool.wait_ge(pool_steps, count)

            in_turn(nc.gpsimd.memset(identity[:, :], 0.0))
            in_turn(nc.gpsimd.memset(parity[:, :], 0.0))
            for i in range(2):
                in_turn(nc.gpsimd.memset(v_blocks[i][:, :, :, :, :], 0.0))
            in_turn(nc.gpsimd.affine_select(out=identity[:, :], in_=identity[:, :], compare_op=ALU.not_equal,
                                            fill=1.0, base=0, pattern=[[-1, 128]], channel_multiplier=1))
            for q in range(4):
                in_turn(nc.gpsimd.memset(parity[32 * q:32 * q + 32, q % 2:q % 2 + 1], 1.0))
            for i in range(2):
                for j in range(2):
                    last = nc.gpsimd.memset(v_blocks[i][64 * j:64 * j + 64, :, :, j, ATT:ATT + 1], 1.0)
                    if (i, j) != (1, 1):
                        in_turn(last)
            last.then_inc(constants, 1)

        @block.tensor
        def _(pe):
            def three_products(psum, w_cols, s, x_cols, x_stationary):
                hi, lo = x_hi[s // 2 % 4], x_lo[s // 2 % 4]
                for n, (w, x) in enumerate(((w_lo, hi), (w_hi, lo), (w_hi, hi))):
                    stationary, moving = w[:, w_cols], x[:, x_cols]
                    if x_stationary:
                        stationary, moving = moving, stationary
                    last = nc.tensor.matmul(psum, stationary, moving, start=(n == 0), stop=(n == 2))
                return last

            def project_qk(turn, s, is_q):
                k = pair(turn, s) * 2 + is_q
                pe.wait_ge(x_split, pair(turn, s) + 1)
                if reaches(pair(turn, s), 1):
                    pe.wait_ge(qk_copied, k - 1)
                for c in range(CHUNKS):
                    col = (1 - is_q) * F + c * 128
                    last = three_products((query_psum if is_q else key_psum)[:, c, :], slice(col, col + 128),
                                          s, slice(0, PAIR), False)
                last.then_inc(qk_projected, 1)

            def scores(turn, s):
                i, u, t = s // 2 % 2, s % 2, tile(turn, s)
                if u == 0:
                    pe.wait_ge(qk_copied, pair(turn, s) * 2 + 2)
                if reaches(t, 1):
                    pe.wait_ge(scores_shifted, t)
                pe.sem_inc(scores_begun, 1)
                for c in range(CHUNKS):
                    for b in range(TB):
                        tok = slice(u * TILE + b * N, u * TILE + b * N + N)
                        for r in range(2):
                            rows = slice(64 * r, 64 * r + 64)
                            last = nc.tensor.matmul(
                                score[64 * b:64 * b + 64, r, 2 * c:2 * c + 2, :],
                                qT[i][rows, c, tok], kT[i][rows, c, :, tok], start=True, stop=True)
                last.then_inc(scored, 1)

            def transposes(turn, s):
                pe.wait_ge(exped, tile(turn, s) + 1)
                for hp in range(HP):
                    c, r = hp // 2, hp % 2
                    last = nc.tensor.transpose(probs_t_bank[:, 128 * hp:128 * hp + 128],
                                               probs[s % 2][:, r, 2 * c:2 * c + 2, :].rearrange("p j m -> p (j m)"),
                                               identity[:, :])
                last.then_inc(transposed, 1)

            def project_v(turn, s):
                t, u = tile(turn, s), s % 2
                if reaches(t, 1):
                    pe.wait_ge(v_copied, t)
                three_products(v_bank[:, 0:F], slice(2 * F, 3 * F), s, slice(u * TILE, u * TILE + TILE),
                               True).then_inc(v_projected, 1)

            def project_res(turn, s):
                t, u = tile(turn, s), s % 2
                if reaches(t, 1):
                    pe.wait_ge(res_added, t)
                three_products(res_bank[:, 0:F], slice(3 * F, 4 * F), s, slice(u * TILE, u * TILE + TILE),
                               True).then_inc(res_projected, 1)

            def attend(turn, s):
                t = tile(turn, s)
                if reaches(t, 1):
                    pe.wait_ge(scaled, t)
                pe.wait_ge(v_copied, t + 1)
                pe.wait_ge(probs_t_copied, t + 1)
                for hp in range(HP):
                    for b in range(TB):
                        last = nc.tensor.matmul(
                            ctx_psum[64 * b:64 * b + 64, 2 * hp:2 * hp + 2, :],
                            probs_t[:, hp, 64 * b:64 * b + 64], v_blocks[s % 2][:, b, hp, :, :],
                            start=True, stop=True)
                last.then_inc(attended, 1)

            def step(turn, s):
                if real(turn, s - 2):
                    transposes(turn, s - 2)
                if real(turn, s):
                    scores(turn, s)
                if real(turn, s + 2):
                    project_qk(turn, s + 2, s % 2)
                if real(turn, s - 1):
                    project_v(turn, s - 1)
                if real(turn, s - 2):
                    project_res(turn, s - 2)
                    attend(turn, s - 2)

            pe.wait_ge(w_split, 1)
            project_qk(0, 0, 0)
            project_qk(0, 0, 1)
            pe.wait_ge(w_split, 2)
            pe.wait_ge(constants, 1)
            run_steps(pe, step)

        @block.scalar
        def _(act):
            def copy_qk(turn, s, is_q):
                q, i = pair(turn, s), s // 2 % 2
                act.wait_ge(qk_projected, q * 2 + (is_q + 1))
                if not is_q and reaches(q, 2):
                    act.wait_ge(scored, q * 2 - 2)
                if is_q:
                    last = nc.scalar.activation(qT[i][:, :, :], query_psum, ACT.Copy)
                else:
                    for j in range(2):
                        last = nc.scalar.activation(kT[i][:, :, j, :], key_psum, ACT.Copy, scale=parity[:, j:j + 1])
                last.then_inc(qk_copied, 1)

            def copy_probs_t(turn, s):
                act.wait_ge(transposed, tile(turn, s) + 1)
                nc.scalar.activation(probs_t[:, :, :], probs_t_bank[:, :].rearrange("p (c n) -> p c n", c=HP),
                                     ACT.Copy).then_inc(probs_t_copied, 1)

            def copy_v(turn, s):
                t = tile(turn, s)
                act.wait_ge(v_projected, t + 1)
                if reaches(t, 2):
                    act.wait_ge(attended, t - 1)
                for b in range(TB):
                    v = v_bank[64 * b:64 * b + 64, 0:F].rearrange("p (c j k) -> p j c k", c=HP, j=2)
                    for j in range(2):
                        last = nc.scalar.activation(v_blocks[s % 2][64 * j:64 * j + 64, b, :, j, 0:ATT],
                                                    v[:, j, :, :], ACT.Copy)
                last.then_inc(v_copied, 1)

            def exp(turn, s):
                act.wait_ge(scores_shifted, tile(turn, s) + 1)
                nc.scalar.activation(probs[s % 2][:, :, :, :], probs[s % 2][:, :, :, :], ACT.Exp,
                                     scale=SCALE).then_inc(exped, 1)

            def step(turn, s):
                if real(turn, s - 2):
                    copy_probs_t(turn, s - 2)
                if real(turn, s + 2):
                    copy_qk(turn, s + 2, s % 2)
                if real(turn, s - 1):
                    copy_v(turn, s - 1)
                if real(turn, s):
                    exp(turn, s)

            act.wait_ge(constants, 1)
            copy_qk(0, 0, 0)
            copy_qk(0, 0, 1)
            run_steps(act, step)

        @block.vector
        def _(dve):
            def split_w(half):
                cols = slice(half * 2 * F, (half + 1) * 2 * F)
                dve.wait_ge(w_loaded[half], 16)
                nc.vector.tensor_copy(w_hi[:, cols], w_in[:, cols]).then_inc(w_rounded, 1)
                dve.wait_ge(w_rounded, half + 1)
                nc.vector.tensor_tensor(w_lo[:, cols], w_in[:, cols], w_hi[:, cols].bitcast(fp32),
                                        ALU.subtract).then_inc(w_split, 1)

            def x_pair(s):
                return x_in[s // GT % 2][:, s // 2 % 2 * PAIR:s // 2 % 2 * PAIR + PAIR]

            def round_x(turn, s):
                q = pair(turn, s)
                dve.wait_ge(x_loaded[s // GT % 2], turn * 16 + (s // BODY) * 16 + 16)
                if reaches(q, 4):
                    dve.wait_ge(res_projected, q * 2 - 6)
                nc.vector.tensor_copy(x_hi[s // 2 % 4][:, :], x_pair(s)).then_inc(x_rounded, 1)

            def rest_x(turn, s):
                dve.wait_ge(x_rounded, pair(turn, s) + 1)
                nc.vector.tensor_tensor(x_lo[s // 2 % 4][:, :], x_pair(s), x_hi[s // 2 % 4][:, :].bitcast(fp32),
                                        ALU.subtract).then_inc(x_split, 1)

            def maxima(turn, s):
                dve.wait_ge(scored, tile(turn, s) + 1)
                nc.vector.tensor_reduce(out=row_max[s % 2][:, :, :], in_=score, axis=AX.X,
                                        op=ALU.max).then_inc(maxed, 1)

            def shift(turn, s):
                dve.wait_ge(maxed, tile(turn, s) + 1)
                nc.vector.tensor_tensor(probs[s % 2][:, :, :, :], score,
                                        row_max[s % 2][:, :, :].unsqueeze(3).to_broadcast([128, 2, H // 2, N]),
                                        ALU.subtract).then_inc(scores_shifted, 1)

            def invert_sums(turn, s):
                dve.wait_ge(attended, tile(turn, s) + 1)
                nc.vector.reciprocal(inv_sum[:, :], ctx_psum[:, :, ATT]).then_inc(inverted, 1)

            def scale_context(turn, s):
                dve.wait_ge(inverted, tile(turn, s) + 1)
                nc.vector.tensor_tensor(head_out[:, :, :], ctx_psum[:, :, 0:ATT],
                                        inv_sum[:, :].unsqueeze(2).to_broadcast([128, H, ATT]),
                                        ALU.mult).then_inc(scaled, 1)

            def add_residual(turn, s):
                t, i, u = tile(turn, s), s // GT % 2, s % GT
                if u == 0 and reaches(t, BODY):
                    dve.wait_ge(stored[i], turn * 16 + (s // BODY) * 16)
                dve.wait_ge(scaled, t + 1)
                dve.wait_ge(res_projected, t + 1)
                nc.vector.tensor_tensor(out_sb[i][:, u, :], res_bank[:, 0:F],
                                        head_out[:, :, :].rearrange("p h k -> p (h k)"),
                                        ALU.add).then_inc(res_added, 1)

            def relu(turn, s):
                o = out_sb[s // GT % 2][:, s % GT, :]
                dve.wait_ge(res_added, tile(turn, s) + 1)
                nc.vector.tensor_scalar(o, o, 0.0, None, ALU.max).then_inc(finished, 1)

            def step(turn, s):
                behind = real(turn, s - 3)
                if behind:
                    invert_sums(turn, s - 3)
                if s % 2 == 0 and real(turn, s + 4):
                    round_x(turn, s + 4)
                if behind:
                    scale_context(turn, s - 3)
                if s % 2 == 1 and real(turn, s + 4):
                    rest_x(turn, s + 4)
                if behind:
                    add_residual(turn, s - 3)
                if real(turn, s):
                    maxima(turn, s)
                if behind:
                    relu(turn, s - 3)
                if real(turn, s):
                    shift(turn, s)

            split_w(0)
            round_x(0, 0)
            rest_x(0, 0)
            split_w(1)
            round_x(0, 2)
            rest_x(0, 2)
            run_steps(dve, step)


def kernel(r_x, L0_rec_W_Q, L0_rec_W_K, L0_rec_W_V, L0_rec_W_res):
    import numpy as np
    import concourse.bacc as bacc
    from concourse.bass_utils import run_bass_kernel_spmd

    B, N, D = r_x.shape
    H, _, ATT = L0_rec_W_Q.shape
    F = H * ATT
    x_t = np.ascontiguousarray(np.asarray(r_x).reshape(B * N, D).transpose(1, 0))
    per_head = [np.asarray(w).transpose(1, 0, 2).reshape(D, F) for w in (L0_rec_W_Q, L0_rec_W_K, L0_rec_W_V)]
    w_t = np.ascontiguousarray(np.concatenate(per_head + [np.asarray(L0_rec_W_res)], axis=1))

    nc = bacc.Bacc("TRN2", target_bir_lowering=False, num_devices=1)
    x_dram = nc.dram_tensor("x_t", x_t.shape, mybir.dt.float32, kind="ExternalInput").ap()
    w_dram = nc.dram_tensor("w_t", w_t.shape, mybir.dt.float32, kind="ExternalInput").ap()
    out_dram = nc.dram_tensor("out", (B * N, F), mybir.dt.float32, kind="ExternalOutput").ap()
    build_attention_program(nc, x_dram, w_dram, out_dram)
    r = run_bass_kernel_spmd(nc, [{"x_t": x_t, "w_t": w_t}], core_ids=[0])
    return r.results[0]["out"].reshape(B, N, F)
```

```python
import concourse.bass as bass
from concourse import mybir
from contextlib import ExitStack


def build_attention_program(nc: bass.Bass, x_t: bass.AP, w_t: bass.AP, out: bass.AP):
    fp32 = mybir.dt.float32
    fp32r = mybir.dt.float32r
    ALU = mybir.AluOpType
    ACT = mybir.ActivationFunctionType
    AX = mybir.AxisListType

    D, TOKENS = x_t.shape
    F = out.shape[1]
    N, ATT = 64, 32
    H = F // ATT
    HP = H // 2
    SCALE = float(ATT) ** -0.5
    TILE = 128
    TB = TILE // N
    PAIR = 2 * TILE
    GT = 4
    GROUP = GT * TILE
    GROUPS = TOKENS // GROUP
    TILES = TOKENS // TILE
    CHUNKS = F // 128
    HC = 128 // ATT
    BLOCK = 32
    QB = TILE // BLOCK
    SP_BLOCKS, POOL_BLOCKS = range(QB - 1), range(QB - 1, QB)
    LAG = 10
    XP = 8
    BODY = 2 * XP
    TURNS = TILES // BODY - 2
    LAST_STEP = TILES - 2 + LAG

    ctx = ExitStack()
    with ctx:
        def sb(name, shape, dt=fp32):
            return ctx.enter_context(nc.sbuf_tensor(name, shape, dt))

        def bank(name):
            return ctx.enter_context(nc.psum_tensor(name, [128, 512], fp32))

        def sem(name):
            return ctx.enter_context(nc.semaphore(name))

        w_in = sb("w_in", [128, 4 * F])
        w_hi = sb("w_hi", [128, 4 * F], fp32r)
        w_lo = sb("w_lo", [128, 4 * F], fp32r)
        x_in = [sb(f"x_in{i}", [128, GROUP]) for i in range(2)]
        x_hi = [sb(f"x_hi{i}", [128, PAIR], fp32r) for i in range(XP)]
        x_lo = [sb(f"x_lo{i}", [128, PAIR], fp32r) for i in range(XP)]
        qT = [sb(f"qT{i}", [128, CHUNKS, PAIR]) for i in range(2)]
        kT = [sb(f"kT{i}", [128, CHUNKS, HC, PAIR]) for i in range(2)]
        row_max = [sb(f"row_max{i}", [128, 2, HP]) for i in range(2)]
        shifted = [sb(f"shifted{i}", [128, 2, 2, HP, BLOCK]) for i in range(2)]
        turned = [sb(f"turned{i}", [128, GT, QB, HP * BLOCK]) for i in range(2)]
        probs_t = [sb(f"probs_t{i}", [128, GT, QB, HP * BLOCK]) for i in range(4)]
        v_blocks = [sb(f"v_blocks{i}", [128, 2, TB, HP, 2, ATT + 1]) for i in range(2)]
        inv_sum = [sb(f"inv_sum{i}", [128, H]) for i in range(2)]
        minus_ctx = [sb(f"minus_ctx{i}", [128, 2, F]) for i in range(2)]
        out_sb = [sb(f"out_sb{i}", [128, GT, F]) for i in range(2)]
        head_rows = sb("head_rows", [128, HC])

        key_bank = bank("key_bank")
        query_bank = bank("query_bank")
        score_bank = [bank(f"score_bank{i}") for i in range(2)]
        v_bank = bank("v_bank")
        res_bank = bank("res_bank")
        ctx_bank = [bank(f"ctx_bank{i}") for i in range(2)]
        key_psum = key_bank[:, :].rearrange("p (c n) -> p c n", c=CHUNKS)
        query_psum = query_bank[:, :].rearrange("p (c n) -> p c n", c=CHUNKS)
        score = [b[:, :].rearrange("p (j kh hp k) -> p j kh hp k", j=2, kh=2, hp=HP) for b in score_bank]
        ctx_psum = [b[:, 0:H * (ATT + 1)].rearrange("p (h e) -> p h e", h=H) for b in ctx_bank]

        w_loaded = [sem(f"w_loaded{i}") for i in range(2)]
        x_loaded = [sem(f"x_loaded{i}") for i in range(2)]
        stored = [sem(f"stored{i}") for i in range(2)]
        pool_steps = sem("pool_steps")
        constants = sem("constants")
        w_rounded = sem("w_rounded")
        w_split = sem("w_split")
        x_rounded = sem("x_rounded")
        x_split = sem("x_split")
        keys_projected = sem("keys_projected")
        queries_projected = sem("queries_projected")
        queries_copied = sem("queries_copied")
        scored = sem("scored")
        maxed = sem("maxed")
        scores_shifted = sem("scores_shifted")
        exped = sem("exped")
        turns_made = sem("turns_made")
        moved = [sem(f"moved{i}") for i in range(2)]
        pool_moved = [sem(f"pool_moved{i}") for i in range(2)]
        v_projected = sem("v_projected")
        v_copied = sem("v_copied")
        res_projected = sem("res_projected")
        attended = sem("attended")
        inverted = sem("inverted")
        scaled = sem("scaled")
        res_maxed = sem("res_maxed")
        finished = sem("finished")

        block = ctx.enter_context(nc.Block())

        def tile(turn, s):
            return turn * BODY + s

        def pair(turn, s):
            return turn * (BODY // 2) + s // 2

        def real(turn, s):
            return not isinstance(turn, int) or 0 <= tile(turn, s) < TILES

        def uses(turn, s):
            return turn * (BODY // (2 * GT)) + s // (2 * GT)

        def reaches(count, least):
            return not isinstance(count, int) or count >= least

        def run_steps(eng, step):
            for s in range(0, BODY, 2):
                step(0, s)
            with eng.Fori(1, TURNS + 1) as turn:
                for s in range(0, BODY, 2):
                    step(turn, s)
            for t in range((TURNS + 1) * BODY, LAST_STEP + 1, 2):
                step(TURNS + 1, t - (TURNS + 1) * BODY)

        def spare_bank(turn, s):
            return isinstance(turn, int) and tile(turn, s) > TILES - LAG + 2

        def res_psum(turn, s):
            return query_bank if spare_bank(turn, s) and s // 2 % 2 else res_bank

        def move_blocks(eng, turn, s, row_blocks, done):
            i = s // GT % 2
            for n in row_blocks:
                for g in range(QB):
                    eng.dma_start(probs_t[s // GT % 4][BLOCK * g:BLOCK * g + BLOCK, :, n, :],
                                  turned[i][BLOCK * n:BLOCK * n + BLOCK, :, g, :]).then_inc(done[i], 16)

        def x_pair(s):
            return x_in[s // GT % 2][:, s // 2 % 2 * PAIR:s // 2 % 2 * PAIR + PAIR]

        @block.sync
        def _(sp):
            def load(turn, s):
                i = s // GT % 2
                g = turn * (BODY // GT) + s // GT
                columns = x_t[:, bass.ds(g * GROUP, GROUP)]
                if reaches(g, 2):
                    sp.wait_ge(x_split, g * 2 - 2)
                sp.dma_start(x_in[i][:, :], columns).then_inc(x_loaded[i], 16)

            def store(turn, s):
                i = s // GT % 2
                g = turn * (BODY // GT) + s // GT
                rows = out[bass.ds(g * GROUP, GROUP), :].rearrange("(t p) f -> p t f", p=TILE)
                sp.wait_ge(finished, g * 2 + 2)
                sp.dma_start(rows, out_sb[i][:, :, :]).then_inc(stored[i], 16)

            def step(turn, s):
                if s % GT == 2 and real(turn, s + 10):
                    load(turn, s + 10)
                if s % GT == 0 and real(turn, s - GT):
                    sp.wait_ge(exped, tile(turn, s))
                    move_blocks(sp, turn, s - GT, SP_BLOCKS, moved)
                if (s - LAG) % GT == 2 and real(turn, s - LAG):
                    store(turn, s - LAG - 2)

            sp.dma_start(w_in[:, 0:2 * F], w_t[:, 0:2 * F]).then_inc(w_loaded[0], 16)
            load(0, 0)
            sp.dma_start(w_in[:, 2 * F:], w_t[:, 2 * F:]).then_inc(w_loaded[1], 16)
            load(0, GT)
            load(0, 2 * GT)
            run_steps(sp, step)
            for i in range(2):
                sp.wait_ge(stored[i], 16 * (GROUPS // 2))

        @block.gpsimd
        def _(pool):
            count = 0

            def in_turn(instruction):
                nonlocal count
                count += 1
                instruction.then_inc(pool_steps, 1)
                pool.wait_ge(pool_steps, count)

            in_turn(nc.gpsimd.memset(head_rows[:, :], 0.0))
            for i in range(2):
                in_turn(nc.gpsimd.memset(v_blocks[i][:, :, :, :, :, :], 0.0))
            for q in range(HC):
                in_turn(nc.gpsimd.memset(head_rows[ATT * q:ATT * q + ATT, q:q + 1], 1.0))
            for i in range(2):
                for j in range(2):
                    last = nc.gpsimd.memset(v_blocks[i][64 * j:64 * j + 64, :, :, :, j, ATT:ATT + 1], -1.0)
                    if (i, j) != (1, 1):
                        in_turn(last)
            last.then_inc(constants, 1)

            def rest_x(turn, s):
                pool.wait_ge(x_rounded, pair(turn, s) + 1)
                nc.gpsimd.tensor_tensor(x_lo[s // 2 % XP][:, :], x_pair(s), x_hi[s // 2 % XP][:, :].bitcast(fp32),
                                        ALU.subtract).then_inc(x_split, 1)

            def finish(turn, s):
                u = s % GT
                o = out_sb[s // GT % 2][:, u:u + 2, :]
                pool.wait_ge(res_maxed, pair(turn, s) + 1)
                nc.gpsimd.tensor_tensor(o, o, minus_ctx[s // 2 % 2][:, :, :], ALU.subtract).then_inc(finished, 1)

            def step(turn, s):
                if real(turn, s + 6):
                    rest_x(turn, s + 6)
                moves = s % GT == 0 and real(turn, s - GT)
                if moves:
                    pool.wait_ge(exped, tile(turn, s))
                if real(turn, s - LAG):
                    finish(turn, s - LAG)
                if moves:
                    move_blocks(pool, turn, s - GT, POOL_BLOCKS, pool_moved)

            pool.wait_ge(constants, 1)
            rest_x(0, 0)
            rest_x(0, 2)
            rest_x(0, 4)
            run_steps(pool, step)

        @block.tensor
        def _(pe):
            def three_products(psum, w_cols, s, x_cols, x_stationary):
                hi, lo = x_hi[s // 2 % XP], x_lo[s // 2 % XP]
                for n, (w, x) in enumerate(((w_lo, hi), (w_hi, lo), (w_hi, hi))):
                    stationary, moving = w[:, w_cols], x[:, x_cols]
                    if x_stationary:
                        stationary, moving = moving, stationary
                    last = nc.tensor.matmul(psum, stationary, moving, start=(n == 0), stop=(n == 2))
                return last

            def project_qk(turn, s, is_q):
                for c in range(CHUNKS):
                    col = (1 - is_q) * F + c * 128
                    last = three_products((query_psum if is_q else key_psum)[:, c, :], slice(col, col + 128),
                                          s, slice(0, PAIR), False)
                last.then_inc(queries_projected if is_q else keys_projected, 1)

            def project_keys_and_queries(turn, s):
                q = pair(turn, s)
                pe.wait_ge(x_split, q + 1)
                if reaches(q, 1):
                    pe.wait_ge(queries_copied, q)
                project_qk(turn, s, False)
                project_qk(turn, s, True)

            def scores(turn, s):
                i, u, t = s // 2 % 2, s % 2, tile(turn, s)
                if u == 0:
                    pe.wait_ge(queries_copied, pair(turn, s) + 1)
                if reaches(t, 2):
                    pe.wait_ge(scores_shifted, t - 1)
                for c in range(CHUNKS):
                    for b in range(TB):
                        tok = slice(u * TILE + b * N, u * TILE + b * N + N)
                        to = score[s % 2][64 * b:64 * b + 64, :, :, 2 * c:2 * c + 2, :].rearrange(
                            "p j kh r k -> p r j kh k")
                        last = nc.tensor.matmul(to, qT[i][:, c, tok], kT[i][:, c, :, tok], start=True, stop=True)
                last.then_inc(scored, 1)

            def project_v(turn, s):
                q = pair(turn, s)
                if reaches(q, 1):
                    pe.wait_ge(v_copied, q)
                for u in range(2):
                    last = three_products(v_bank[:, u * F:u * F + F], slice(2 * F, 3 * F), s,
                                          slice(u * TILE, u * TILE + TILE), True)
                last.then_inc(v_projected, 1)

            def project_res(turn, s):
                q, to = pair(turn, s), res_psum(turn, s)
                if reaches(q, 1):
                    pe.wait_ge(res_maxed, q - 1 if spare_bank(turn, s) else q)
                for u in range(2):
                    last = three_products(to[:, u * F:u * F + F], slice(3 * F, 4 * F), s,
                                          slice(u * TILE, u * TILE + TILE), True)
                last.then_inc(res_projected, 1)

            def attend(turn, s):
                t, u = tile(turn, s), s % 2
                if reaches(t, 2):
                    pe.wait_ge(scaled, t - 1)
                if u == 0:
                    pe.wait_ge(v_copied, pair(turn, s) + 1)
                if s % GT == 0:
                    pe.wait_ge(moved[s // GT % 2], (uses(turn, s) + 1) * (16 * QB * len(SP_BLOCKS)))
                    pe.wait_ge(pool_moved[s // GT % 2], (uses(turn, s) + 1) * (16 * QB * len(POOL_BLOCKS)))
                for hp in range(HP):
                    for n in range(QB):
                        last = nc.tensor.matmul(
                            ctx_psum[u][BLOCK * n:BLOCK * n + BLOCK, 2 * hp:2 * hp + 2, :],
                            probs_t[s // GT % 4][:, s % GT, n, BLOCK * hp:BLOCK * hp + BLOCK],
                            v_blocks[s // 2 % 2][:, u, n // 2, hp, :, :], start=True, stop=True)
                last.then_inc(attended, 1)

            def step(turn, s):
                if real(turn, s - LAG):
                    attend(turn, s - LAG)
                    attend(turn, s - LAG + 1)
                keys_first = isinstance(turn, int) and 0 < tile(turn, s) < LAG
                if keys_first:
                    project_keys_and_queries(turn, s + 2)
                if real(turn, s):
                    scores(turn, s)
                    scores(turn, s + 1)
                if real(turn, s + 2) and not keys_first:
                    project_keys_and_queries(turn, s + 2)
                if real(turn, s - LAG + 4):
                    project_v(turn, s - LAG + 4)
                if real(turn, s - LAG + 2):
                    project_res(turn, s - LAG + 2)

            pe.wait_ge(w_split, 1)
            project_keys_and_queries(0, 0)
            pe.wait_ge(w_split, 2)
            run_steps(pe, step)

        @block.scalar
        def _(act):
            def copy_keys(turn, s):
                q, i = pair(turn, s), s // 2 % 2
                act.wait_ge(keys_projected, q + 1)
                if reaches(q, 2):
                    act.wait_ge(scored, q * 2 - 2)
                for h in range(HC):
                    nc.scalar.activation(kT[i][:, :, h, :], key_psum, ACT.Copy, scale=head_rows[:, h:h + 1])

            def copy_queries(turn, s):
                act.wait_ge(queries_projected, pair(turn, s) + 1)
                nc.scalar.activation(qT[s // 2 % 2][:, :, :], query_psum, ACT.Copy).then_inc(queries_copied, 1)

            def round_x(turn, s):
                q = pair(turn, s)
                act.wait_ge(x_loaded[s // GT % 2], uses(turn, s) * 16 + 16)
                if reaches(q, XP):
                    act.wait_ge(res_projected, q - XP + 1)
                nc.scalar.activation(x_hi[s // 2 % XP][:, :], x_pair(s), ACT.Copy).then_inc(x_rounded, 1)

            def copy_v(turn, s):
                q = pair(turn, s)
                act.wait_ge(v_projected, q + 1)
                if reaches(q, 2):
                    act.wait_ge(attended, q * 2 - 2)
                for b in range(TB):
                    v = v_bank[64 * b:64 * b + 64, :].rearrange("p (u c j k) -> p u j c k", u=2, c=HP, j=2)
                    for j in range(2):
                        last = nc.scalar.activation(v_blocks[s // 2 % 2][64 * j:64 * j + 64, :, b, :, j, 0:ATT],
                                                    v[:, :, j, :, :], ACT.Copy)
                last.then_inc(v_copied, 1)

            def exp(turn, s):
                t = tile(turn, s)
                act.wait_ge(turns_made, t + 1)
                probs = turned[s // GT % 2][:, s % GT, :, :]
                nc.scalar.activation(probs, probs, ACT.Exp,
                                     scale=SCALE).then_inc(exped, 1)

            def step(turn, s):
                if real(turn, s + 6):
                    round_x(turn, s + 6)
                keys_first = isinstance(turn, int) and tile(turn, s) < LAG - 2
                if keys_first:
                    if real(turn, s + 2):
                        copy_keys(turn, s + 2)
                        copy_queries(turn, s + 2)
                if real(turn, s - 2):
                    exp(turn, s - 2)
                    exp(turn, s - 1)
                if real(turn, s - LAG + 2):
                    copy_v(turn, s - LAG + 2)
                if real(turn, s + 2) and not keys_first:
                    copy_keys(turn, s + 2)
                    copy_queries(turn, s + 2)

            round_x(0, 0)
            round_x(0, 2)
            act.wait_ge(constants, 1)
            copy_keys(0, 0)
            copy_queries(0, 0)
            round_x(0, 4)
            run_steps(act, step)

        @block.vector
        def _(dve):
            def split_w(half):
                cols = slice(half * 2 * F, (half + 1) * 2 * F)
                dve.wait_ge(w_loaded[half], 16)
                nc.vector.tensor_copy(w_hi[:, cols], w_in[:, cols]).then_inc(w_rounded, 1)
                dve.wait_ge(w_rounded, half + 1)
                nc.vector.tensor_tensor(w_lo[:, cols], w_in[:, cols], w_hi[:, cols].bitcast(fp32),
                                        ALU.subtract).then_inc(w_split, 1)

            def maxima(turn, s):
                dve.wait_ge(scored, tile(turn, s) + 1)
                nc.vector.tensor_reduce(out=row_max[s % 2][:, :, :],
                                        in_=score[s % 2].rearrange("p j kh hp k -> p j hp kh k"),
                                        axis=AX.XY, op=ALU.max).then_inc(maxed, 1)

            def shift(turn, s):
                dve.wait_ge(maxed, tile(turn, s) + 1)
                for j in range(2):
                    most = row_max[s % 2][:, j, :].unsqueeze(1).unsqueeze(3).to_broadcast([128, 2, HP, BLOCK])
                    last = nc.vector.tensor_tensor(shifted[s % 2][:, j, :, :, :], score[s % 2][:, j, :, :, :], most,
                                                   ALU.subtract)
                last.then_inc(scores_shifted, 1)

            def turn_blocks(turn, s):
                t = tile(turn, s)
                dve.wait_ge(scores_shifted, t + 1)
                if s % GT == 0 and reaches(t, 2 * GT):
                    dve.wait_ge(moved[s // GT % 2], uses(turn, s) * (16 * QB * len(SP_BLOCKS)))
                    dve.wait_ge(pool_moved[s // GT % 2], uses(turn, s) * (16 * QB * len(POOL_BLOCKS)))
                nc.vector.transpose(turned[s // GT % 2][:, s % GT, :, :].rearrange("p g c -> p (g c)"),
                                    shifted[s % 2][:, :, :, :, :].rearrange("p j kh hp k -> p (j kh hp k)"))\
                    .then_inc(turns_made, 1)

            def invert_sums(turn, s):
                dve.wait_ge(attended, tile(turn, s) + 1)
                nc.vector.reciprocal(inv_sum[s % 2][:, :], ctx_psum[s % 2][:, :, ATT]).then_inc(inverted, 1)

            def scale_context(turn, s):
                t, u = tile(turn, s), s % 2
                if u == 0 and reaches(t, 4):
                    dve.wait_ge(finished, pair(turn, s) - 1)
                dve.wait_ge(inverted, t + 1)
                nc.vector.tensor_tensor(minus_ctx[s // 2 % 2][:, u, :].rearrange("p (h k) -> p h k", h=H),
                                        ctx_psum[u][:, :, 0:ATT],
                                        inv_sum[u][:, :].unsqueeze(2).to_broadcast([128, H, ATT]),
                                        ALU.mult).then_inc(scaled, 1)

            def max_residual(turn, s):
                t, i, u = tile(turn, s), s // GT % 2, s % GT
                if u == 0 and reaches(t, 2 * GT):
                    dve.wait_ge(stored[i], uses(turn, s) * 16)
                dve.wait_ge(scaled, t + 2)
                dve.wait_ge(res_projected, pair(turn, s) + 1)
                nc.vector.tensor_tensor(out_sb[i][:, u:u + 2, :].rearrange("p t f -> p (t f)"),
                                        res_psum(turn, s)[:, :],
                                        minus_ctx[s // 2 % 2][:, :, :].rearrange("p t f -> p (t f)"),
                                        ALU.max).then_inc(res_maxed, 1)

            def step(turn, s):
                behind = real(turn, s - LAG)
                if behind:
                    invert_sums(turn, s - LAG)
                    invert_sums(turn, s - LAG + 1)
                    scale_context(turn, s - LAG)
                    scale_context(turn, s - LAG + 1)
                if real(turn, s):
                    maxima(turn, s)
                if behind:
                    max_residual(turn, s - LAG)
                if real(turn, s):
                    shift(turn, s)
                    maxima(turn, s + 1)
                    turn_blocks(turn, s)
                    shift(turn, s + 1)
                    turn_blocks(turn, s + 1)

            split_w(0)
            split_w(1)
            run_steps(dve, step)


def kernel(r_x, L0_rec_W_Q, L0_rec_W_K, L0_rec_W_V, L0_rec_W_res):
    import numpy as np
    import concourse.bacc as bacc
    from concourse.bass_utils import run_bass_kernel_spmd

    B, N, D = r_x.shape
    H, _, ATT = L0_rec_W_Q.shape
    F = H * ATT
    x_t = np.ascontiguousarray(np.asarray(r_x).reshape(B * N, D).transpose(1, 0))
    per_head = [np.asarray(w).transpose(1, 0, 2).reshape(D, F) for w in (L0_rec_W_Q, L0_rec_W_K, L0_rec_W_V)]
    w_t = np.ascontiguousarray(np.concatenate(per_head + [np.asarray(L0_rec_W_res)], axis=1))

    nc = bacc.Bacc("TRN2", target_bir_lowering=False, num_devices=1)
    x_dram = nc.dram_tensor("x_t", x_t.shape, mybir.dt.float32, kind="ExternalInput").ap()
    w_dram = nc.dram_tensor("w_t", w_t.shape, mybir.dt.float32, kind="ExternalInput").ap()
    out_dram = nc.dram_tensor("out", (B * N, F), mybir.dt.float32, kind="ExternalOutput").ap()
    build_attention_program(nc, x_dram, w_dram, out_dram)
    r = run_bass_kernel_spmd(nc, [{"x_t": x_t, "w_t": w_t}], core_ids=[0])
    return r.results[0]["out"].reshape(B, N, F)
```
